# Optimizing a Trainium2 kernel written in Bass

```python
import numpy as np
import jax
import jax.numpy as jnp

def _softmax(x, axis=-1):
    return jax.nn.softmax(x, axis=axis)

def _gelu(x):
    return jax.nn.gelu(x, approximate=True)

def _silu(x):
    return jax.nn.silu(x)

def _sigmoid(x):
    return jax.nn.sigmoid(x)

def _layernorm(x, axis=-1, eps=1e-05):
    m = jnp.mean(x, axis=axis, keepdims=True)
    v = jnp.var(x, axis=axis, keepdims=True)
    return (x - m) / jnp.sqrt(v + eps)

def _scatter_add(tgt, idx, src, axis=0):
    return tgt.at[idx].add(src)

def _segment_sum(src, seg, n):
    return jax.ops.segment_sum(src, seg, n)
kernel_name = 'mk_rec_standalone_d1_rec_r8_5fa24f'

def setup_inputs(seed: int=0):
    np.random.seed(seed)
    _w = jnp.asarray

    def _rec_inputs():
        import jax
        import jax.numpy as jnp
        _rk = jax.random.key(seed)
        r_x = -0.000520686 + 1.00062 * jax.random.normal(jax.random.fold_in(_rk, 1), (2048, 2, 1024), jnp.float32)
        return r_x
    r_x = _rec_inputs()

    def _L0_rec_setup():
        import jax, jax.numpy as jnp
        import numpy as np
        B, L, D, F = (1024, 2, 1024, 4096)
        key = jax.random.key(seed)
        k1, k2, k3 = jax.random.split(key, 3)
        scale = 1.0 / np.sqrt(D)
        x = jax.random.normal(k1, (B, L, D), dtype=jnp.float32)
        W_enc = jax.random.normal(k2, (L, D, F), dtype=jnp.float32) * scale
        b_enc = jnp.zeros((F,), dtype=jnp.float32)
        W_dec = jax.random.normal(k3, (L, F, D), dtype=jnp.float32) * scale
        b_dec = jnp.zeros((L, D), dtype=jnp.float32)
        return {'x': x, 'W_enc': W_enc, 'b_enc': b_enc, 'W_dec': W_dec, 'b_dec': b_dec}
    _L0_rec_all = _L0_rec_setup()
    _L0_rec_in = {k: v for k, v in _L0_rec_all.items() if k in ('W_enc', 'b_enc', 'W_dec', 'b_dec')}
    del _L0_rec_all
    return {'r_x': r_x, 'L0_rec_W_enc': _L0_rec_in['W_enc'], 'L0_rec_b_enc': _L0_rec_in['b_enc'], 'L0_rec_W_dec': _L0_rec_in['W_dec'], 'L0_rec_b_dec': _L0_rec_in['b_dec']}

def reference(r_x, L0_rec_W_enc, L0_rec_b_enc, L0_rec_W_dec, L0_rec_b_dec):
    import jax
    import jax.numpy as jnp

    def _L0_rec_ref(x, W_enc, b_enc, W_dec, b_dec):
        import jax, jax.numpy as jnp
        import numpy as np
        B, L, D, F = (1024, 2, 1024, 4096)
        f = jax.nn.relu(jnp.einsum('bld,ldf->bf', x, W_enc) + b_enc)
        x_hat = jnp.einsum('bf,lfd->bld', f, W_dec) + b_dec
        return x_hat
    y = _L0_rec_ref(r_x, L0_rec_W_enc, L0_rec_b_enc, L0_rec_W_dec, L0_rec_b_dec)
    return y

_drawn_inputs = setup_inputs


def setup_inputs(seed=0):
    import zlib

    import numpy as np

    out = dict(_drawn_inputs(seed))
    spreads = {'L0_rec_b_enc': (0.0, 0.1), 'L0_rec_b_dec': (0.0, 0.1)}
    factors = {}
    for name, (base, spread) in spreads.items():
        noise = np.random.default_rng([zlib.crc32(name.encode()), seed]).standard_normal(out[name].shape)
        drawn = base * np.exp(spread * noise) if base else spread * noise
        out[name] = jnp.asarray(drawn.astype(out[name].dtype))
    for name, factor in factors.items():
        out[name] = (out[name] * factor).astype(out[name].dtype)
    return out
```

```python
from contextlib import ExitStack

import concourse.bass as bass
from concourse import mybir

P = 128
ROWS, LAYERS, WIDTH, F = 2048, 2, 1024, 4096
D = LAYERS * WIDTH
N = 512
BLOCKS = ROWS // N
ROW_TILES = N // P
K_TILES = D // P
GROUP = 8
GROUPS = F // P // GROUP
CHUNKS = D // N
UNIT = K_TILES * P
DEC_TILES = UNIT // N
X_TILES = UNIT // N
X_UNITS = K_TILES // X_TILES
PER_CHUNK = GROUP // DEC_TILES
ENC_UNITS = GROUP
DEC_UNITS = CHUNKS * PER_CHUNK
G_UNITS = ENC_UNITS + DEC_UNITS
B_UNITS = GROUPS * G_UNITS

RAW = 2
SLOTS = 2
LATENT_BANKS = 2
OUT_BANKS = ROW_TILES
QUARTERS = 4


def build(nc, xT, w_enc, b_enc, w_dec, b_dec, out):
    f32, f32r = mybir.dt.float32, mybir.dt.float32r
    ALU, ACT = mybir.AluOpType, mybir.ActivationFunctionType

    with ExitStack() as ctx:
        def sb(name, shape, dt=f32):
            return ctx.enter_context(nc.sbuf_tensor(name, shape, dt))

        def sem(name):
            return ctx.enter_context(nc.semaphore(name))

        x_hi = sb("x_hi", [P, K_TILES, N], f32r)
        x_lo = sb("x_lo", [P, K_TILES, N], f32r)
        f_hi = sb("f_hi", [P, GROUP, N], f32r)
        f_lo = sb("f_lo", [P, GROUP, N], f32r)
        w_hi = sb("w_hi", [P, SLOTS, UNIT], f32r)
        w_lo = sb("w_lo", [P, SLOTS, UNIT], f32r)
        w_raw = sb("w_raw", [P, RAW, UNIT])
        x_raw = sb("x_raw", [P, UNIT])
        latent = sb("latent", [P, LATENT_BANKS, N])
        out_sum = sb("out_sum", [P, ROW_TILES, D])
        b_dec_rows = sb("b_dec_rows", [P, D])
        b_enc_cols = sb("b_enc_cols", [P, F // P])
        latent_ps = [ctx.enter_context(nc.psum_tensor(f"latent_ps{i}", [P, N], f32))
                     for i in range(LATENT_BANKS)]
        out_ps = [ctx.enter_context(nc.psum_tensor(f"out_ps{i}", [P, N], f32)) for i in range(OUT_BANKS)]

        w_loaded = [sem(f"w_loaded{i}") for i in range(RAW)]
        x_first_loaded = [sem(f"x_first_loaded{i}") for i in range(X_UNITS)]
        x_loaded = sem("x_loaded")
        b_enc_loaded = sem("b_enc_loaded")
        b_dec_loaded = sem("b_dec_loaded")
        out_stored = sem("out_stored")
        w_hi_made = sem("w_hi_made")
        w_split = sem("w_split")
        x_hi_made = sem("x_hi_made")
        x_split = sem("x_split")
        quarters = sem("quarters")
        latent_made = sem("latent_made")
        latent_split = sem("latent_split")
        out_added = sem("out_added")
        out_free = sem("out_free")

        def raw_free(u):
            return u - RAW + 1 + RAW

        def split_done(u):
            return u + 1 + RAW

        def quarter_done(u, q):
            return QUARTERS * u + q + 1 + QUARTERS * SLOTS

        def unit_used(u):
            return quarter_done(u, QUARTERS - 1)

        def w_slot_free(u):
            return unit_used(u - SLOTS)

        def x_part(buf, c):
            return buf[:, c * X_TILES:(c + 1) * X_TILES, :].rearrange("p k n -> p (k n)")

        block = ctx.enter_context(nc.Block())

        @block.sync
        def _(sp):
            with sp.Fori(0, BLOCKS) as b:
                with sp.Fori(0, GROUPS) as g:
                    for part, (w, count) in enumerate(((w_enc, ENC_UNITS), (w_dec, DEC_UNITS))):
                        with sp.Fori(0, count // RAW) as n:
                            for s in range(RAW):
                                i = n * RAW + s
                                u = b * B_UNITS + g * G_UNITS + part * ENC_UNITS + i
                                sp.wait_ge(w_split, raw_free(u))
                                sp.dma_start(w_raw[:, s, :], w[g * count + i, :, :],
                                             max_dma_last_dim=UNIT * 4).then_inc(w_loaded[s], 16)

        @block.gpsimd
        def _(pool):
            pool.sem_inc(out_free, 1)
            pool.dma_start(b_dec_rows[:, :], b_dec.partition_broadcast(P)).then_inc(b_dec_loaded, 16)
            with pool.Fori(0, BLOCKS) as b:
                rows = out[bass.ds(b * N, N), :].rearrange("(r p) d -> p r d", p=P)
                for c in range(CHUNKS):
                    done = b * (GROUPS * CHUNKS) + (GROUPS - 1) * CHUNKS + c + 1
                    pool.wait_ge(out_added, done * OUT_BANKS + OUT_BANKS)
                    pool.dma_start(rows[:, :, c * N:(c + 1) * N], out_sum[:, :, c * N:(c + 1) * N])\
                        .then_inc(out_stored, 16)
                pool.wait_ge(out_stored, b * (16 * CHUNKS) + 16 * CHUNKS)
                pool.sem_inc(out_free, 1)

        @block.scalar
        def _(act):
            def load_x(b, c):
                act.dma_start(x_raw[:, :], xT[b, c, :, :], max_dma_last_dim=UNIT * 4).then_inc(x_loaded, 16)

            def make_w_hi(b, g, i):
                u = b * B_UNITS + g * G_UNITS + i
                act.wait_ge(w_loaded[i % RAW], (b * B_UNITS + g * G_UNITS + i - i % RAW) * (16 // RAW) + 16)
                act.wait_ge(quarters, w_slot_free(u))
                act.activation(w_hi[:, i % SLOTS, :], w_raw[:, i % RAW, :], ACT.Copy).then_inc(w_hi_made, 1)

            def make_latent(b, g, i):
                t = b * (GROUPS * GROUP) + g * GROUP + i
                s = i % LATENT_BANKS
                act.wait_ge(quarters, unit_used(b * B_UNITS + g * G_UNITS + i))
                act.wait_ge(latent_split, t + 1)
                bias = b_enc_cols[:, bass.ds(g * GROUP + i, 1)]
                act.activation(latent[:, s, :], latent_ps[s][:, :], ACT.Relu, bias=bias)
                act.activation(f_hi[:, i, :], latent_ps[s][:, :], ACT.Relu, bias=bias)\
                    .then_inc(latent_made, 1)

            def make_x_hi(c, src):
                act.activation(x_part(x_hi, c), src, ACT.Copy).then_inc(x_hi_made, 1)

            def group(b, g, prepare_x):
                for i in range(G_UNITS):
                    make_w_hi(b, g, i)
                    if 1 <= i <= GROUP:
                        make_latent(b, g, i - 1)
                    if not prepare_x:
                        continue
                    c, odd = divmod(i - ENC_UNITS, PER_CHUNK)
                    if i == 0 or (c >= 1 and not odd):
                        c = max(c, 0)
                        act.wait_ge(x_split, b * X_UNITS + X_UNITS + c)
                        load_x(b + 1, c)
                    elif c >= 0 and odd:
                        act.wait_ge(x_loaded, b * (16 * X_UNITS) + 16 * (c + 1))
                        make_x_hi(c, x_raw[:, :])

            act.sem_inc(latent_made, LATENT_BANKS)
            for c in range(X_UNITS):
                act.dma_start(out_sum[:, c, :], xT[0, c, :, :], max_dma_last_dim=UNIT * 4)\
                    .then_inc(x_first_loaded[c], 16)
            act.dma_start(b_enc_cols[:, :], b_enc[:, :]).then_inc(b_enc_loaded, 16)
            for c in range(X_UNITS):
                act.wait_ge(x_first_loaded[c], 16)
                make_x_hi(c, out_sum[:, c, :])
            act.wait_ge(b_enc_loaded, 16)
            with act.Fori(0, BLOCKS - 1) as b:
                with act.Fori(0, GROUPS - 1) as g:
                    group(b, g, prepare_x=False)
                group(b, GROUPS - 1, prepare_x=True)
            with act.Fori(0, GROUPS) as g:
                group(BLOCKS - 1, g, prepare_x=False)

        @block.vector
        def _(dve):
            def make_w_lo(b, g, i):
                dve.wait_ge(w_hi_made, b * B_UNITS + g * G_UNITS + i + 1)
                s, r = i % SLOTS, i % RAW
                dve.tensor_tensor(w_lo[:, s, :], w_raw[:, r, :], w_hi[:, s, :].bitcast(f32), ALU.subtract)\
                    .then_inc(w_split, 1)

            def split_latent(b, g, i):
                dve.wait_ge(latent_made, b * (GROUPS * GROUP) + g * GROUP + i + 1 + LATENT_BANKS)
                dve.tensor_tensor(f_lo[:, i, :], latent[:, i % LATENT_BANKS, :], f_hi[:, i, :].bitcast(f32),
                                  ALU.subtract).then_inc(latent_split, 1)

            def split_x(b, c, src):
                dve.wait_ge(x_hi_made, b * X_UNITS + c + 1)
                dve.tensor_tensor(x_part(x_lo, c), src, x_part(x_hi, c).bitcast(f32), ALU.subtract)\
                    .then_inc(x_split, 1)

            def add_chunk(b, g, c, first):
                u = b * B_UNITS + g * G_UNITS + ENC_UNITS + (c + 1) * PER_CHUNK - 1
                cols = slice(c * N, (c + 1) * N)
                if first and c == 0:
                    dve.wait_ge(out_free, b + 1)
                for r in range(ROW_TILES):
                    dve.wait_ge(quarters, quarter_done(u, r))
                    onto = b_dec_rows[:, cols] if first else out_sum[:, r, cols]
                    dve.tensor_tensor(out_sum[:, r, cols], out_ps[r][:, :], onto, ALU.add)\
                        .then_inc(out_added, 1)

            def group(b, g, first=False, prepare_x=False, ends=False):
                for i in range(G_UNITS):
                    if not (ends and i == G_UNITS - 1):
                        make_w_lo(b, g, i + 1)
                    if i < ENC_UNITS:
                        split_latent(b, g, i)
                        continue
                    c, odd = divmod(i - ENC_UNITS, PER_CHUNK)
                    if odd:
                        add_chunk(b, g, c, first)
                    elif prepare_x:
                        split_x(b + 1, c, x_raw[:, :])

            dve.sem_inc(w_split, RAW)
            dve.sem_inc(latent_split, LATENT_BANKS)
            dve.sem_inc(out_added, OUT_BANKS)
            for c in range(X_UNITS):
                split_x(0, c, out_sum[:, c, :])
            make_w_lo(0, 0, 0)
            dve.wait_ge(b_dec_loaded, 16)
            with dve.Fori(0, BLOCKS - 1) as b:
                group(b, 0, first=True)
                with dve.Fori(1, GROUPS - 1) as g:
                    group(b, g)
                group(b, GROUPS - 1, prepare_x=True)
            group(BLOCKS - 1, 0, first=True)
            with dve.Fori(1, GROUPS - 1) as g:
                group(BLOCKS - 1, g)
            group(BLOCKS - 1, GROUPS - 1, ends=True)

        @block.tensor
        def _(pe):
            def products(ps, a_hi, a_lo, b_hi, b_lo, start, stop):
                pe.matmul(ps, a_hi, b_hi, start=start, stop=False)
                pe.matmul(ps, a_hi, b_lo, start=False, stop=False)
                return pe.matmul(ps, a_lo, b_hi, start=False, stop=stop)

            def encode(b, g, i, j):
                t = b * (GROUPS * GROUP) + g * GROUP + i
                pe.wait_ge(w_split, split_done(b * B_UNITS + g * G_UNITS + i))
                pe.wait_ge(latent_made, t + 1)
                for k in range(K_TILES):
                    if j == 0 and k % X_TILES == 0:
                        pe.wait_ge(x_split, b * X_UNITS + k // X_TILES + 1)
                    w = slice(k * P, (k + 1) * P)
                    last = products(latent_ps[j][:, :], w_hi[:, j, w], w_lo[:, j, w],
                                    x_hi[:, k, :], x_lo[:, k, :], k == 0, k == K_TILES - 1)
                    if (k + 1) % (K_TILES // QUARTERS) == 0:
                        last.then_inc(quarters, 1)

            def decode(b, g, c, h):
                pe.wait_ge(w_split, split_done(b * B_UNITS + g * G_UNITS + ENC_UNITS + c * PER_CHUNK + h))
                for r in range(ROW_TILES):
                    if h == 0:
                        pe.wait_ge(out_added, ((b * GROUPS + g) * CHUNKS + c) * OUT_BANKS + r + 1)
                    for t in range(DEC_TILES):
                        ft = h * DEC_TILES + t
                        if r == 0:
                            pe.wait_ge(latent_split, (b * GROUPS + g) * GROUP + ft + 1 + LATENT_BANKS)
                        w, rows = slice(t * N, (t + 1) * N), slice(r * P, (r + 1) * P)
                        last = products(out_ps[r][:, :], f_hi[:, ft, rows], f_lo[:, ft, rows],
                                        w_hi[:, h, w], w_lo[:, h, w], ft == 0, ft == GROUP - 1)
                    last.then_inc(quarters, 1)

            pe.sem_inc(quarters, QUARTERS * SLOTS)
            with pe.Fori(0, BLOCKS) as b:
                with pe.Fori(0, GROUPS) as g:
                    with pe.Fori(0, ENC_UNITS // SLOTS) as n:
                        for j in range(SLOTS):
                            encode(b, g, n * SLOTS + j, j)
                    with pe.Fori(0, CHUNKS) as c:
                        for h in range(PER_CHUNK):
                            decode(b, g, c, h)


def kernel(r_x, L0_rec_W_enc, L0_rec_b_enc, L0_rec_W_dec, L0_rec_b_dec):
    import numpy as np
    import concourse.bacc as bacc
    from concourse.bass_utils import run_bass_kernel_spmd

    def packed(a):
        return np.ascontiguousarray(a)

    x = np.asarray(r_x).reshape(BLOCKS, N, X_UNITS, X_TILES, P)
    we = np.asarray(L0_rec_W_enc).reshape(K_TILES, P, F // P, P)
    wd = np.asarray(L0_rec_W_dec).transpose(1, 0, 2).reshape(GROUPS, PER_CHUNK, DEC_TILES, P, CHUNKS, N)
    arrays = {
        "xT": packed(x.transpose(0, 2, 4, 3, 1)).reshape(BLOCKS, X_UNITS, P, UNIT),
        "w_enc": packed(we.transpose(2, 1, 0, 3)).reshape(GROUPS * ENC_UNITS, P, UNIT),
        "b_enc": packed(np.asarray(L0_rec_b_enc).reshape(F // P, P).T),
        "w_dec": packed(wd.transpose(0, 4, 1, 3, 2, 5)).reshape(GROUPS * DEC_UNITS, P, UNIT),
        "b_dec": packed(np.asarray(L0_rec_b_dec).reshape(D)),
    }
    nc = bacc.Bacc("TRN2", target_bir_lowering=False, num_devices=1)
    args = [nc.dram_tensor(name, a.shape, mybir.dt.from_np(a.dtype), kind="ExternalInput").ap()
            for name, a in arrays.items()]
    args.append(nc.dram_tensor("x_hat", [ROWS, D], mybir.dt.float32, kind="ExternalOutput").ap())
    build(nc, *args)
    got = run_bass_kernel_spmd(nc, [arrays], core_ids=[0])
    return got.results[0]["x_hat"].reshape(ROWS, LAYERS, WIDTH)
```

```python
from contextlib import ExitStack

import concourse.bass as bass
from concourse import mybir

P = 128
ROWS, LAYERS, WIDTH, F = 2048, 2, 1024, 4096
D = LAYERS * WIDTH
N = 512
BLOCKS = ROWS // N
ROW_TILES = N // P
K_TILES = D // P
GROUP = 8
GROUPS = F // P // GROUP
CHUNKS = D // N
UNIT = K_TILES * P
DEC_TILES = UNIT // N
X_TILES = UNIT // N
X_UNITS = K_TILES // X_TILES
PER_CHUNK = GROUP // DEC_TILES
ENC_UNITS = GROUP
DEC_UNITS = CHUNKS * PER_CHUNK
G_UNITS = ENC_UNITS + DEC_UNITS
B_UNITS = GROUPS * G_UNITS

RAW = 2
SLOTS = 2
LATENT_BANKS = 2
OUT_BANKS = ROW_TILES
FIRST = [(k, k + 1) for k in range(X_TILES)] + [(k, k + 2) for k in range(X_TILES, K_TILES, 2)]
QUARTERS = 4


def build(nc, xT, w_enc, b_enc, w_dec, b_dec, out):
    f32, f32r = mybir.dt.float32, mybir.dt.float32r
    ALU, ACT = mybir.AluOpType, mybir.ActivationFunctionType

    with ExitStack() as ctx:
        def sb(name, shape, dt=f32):
            return ctx.enter_context(nc.sbuf_tensor(name, shape, dt))

        def sem(name):
            return ctx.enter_context(nc.semaphore(name))

        x_hi = sb("x_hi", [P, K_TILES, N], f32r)
        x_lo = sb("x_lo", [P, K_TILES, N], f32r)
        f_hi = sb("f_hi", [P, GROUP, N], f32r)
        f_lo = sb("f_lo", [P, GROUP, N], f32r)
        w_hi = sb("w_hi", [P, SLOTS, UNIT], f32r)
        w_lo = sb("w_lo", [P, SLOTS, UNIT], f32r)
        w_raw = sb("w_raw", [P, RAW, UNIT])
        staging = sb("staging", [P, SLOTS, UNIT])
        x_raw, b_dec_rows = staging[:, 0, :], staging[:, 1, :]
        latent = sb("latent", [P, LATENT_BANKS, N])
        out_sum = sb("out_sum", [P, ROW_TILES, D])
        b_enc_cols = sb("b_enc_cols", [P, F // P])
        latent_ps = [ctx.enter_context(nc.psum_tensor(f"latent_ps{i}", [P, N], f32))
                     for i in range(LATENT_BANKS)]
        out_ps = [ctx.enter_context(nc.psum_tensor(f"out_ps{i}", [P, N], f32)) for i in range(OUT_BANKS)]

        w_first_loaded = [sem(f"w_first_loaded{i}") for i in range(len(FIRST))]
        x_first_loaded = [sem(f"x_first_loaded{i}") for i in range(len(FIRST))]
        w_loaded = [sem(f"w_loaded{i}") for i in range(RAW)]
        x_loaded = sem("x_loaded")
        b_enc_loaded = sem("b_enc_loaded")
        b_dec_loaded = sem("b_dec_loaded")
        out_stored = sem("out_stored")
        last_stored = sem("last_stored")
        first_hi_made = sem("first_hi_made")
        first_split = sem("first_split")
        w_hi_made = sem("w_hi_made")
        w_split = sem("w_split")
        x_hi_made = sem("x_hi_made")
        x_split = sem("x_split")
        quarters = sem("quarters")
        latent_made = sem("latent_made")
        latent_split = sem("latent_split")
        out_added = sem("out_added")
        out_free = sem("out_free")

        def unit(b, g, i):
            return b * B_UNITS + g * G_UNITS + i

        def raw_free(u):
            return u - RAW + 1

        def quarter_used(u, q):
            return u * QUARTERS + q + 1

        def unit_used(u):
            return quarter_used(u, QUARTERS - 1)

        def tiles_added(b, g, c):
            return ((b * GROUPS + g) * CHUNKS + c) * ROW_TILES + OUT_BANKS

        def x_part(buf, c):
            return buf[:, c * X_TILES:(c + 1) * X_TILES, :].rearrange("p k n -> p (k n)")

        def first_pieces():
            for n, (k, end) in enumerate(FIRST):
                w = slice(k * P, end * P)
                yield (w_hi[:, :, w], w_lo[:, :, w], staging[:, :, w],
                       w_enc[0:SLOTS, :, w].rearrange("t p n -> p t n"), w_first_loaded[n])
                c, x = k // X_TILES, slice(k % X_TILES * N, (k % X_TILES + end - k) * N)
                yield (x_part(x_hi, c)[:, x], x_part(x_lo, c)[:, x], out_sum[:, c, x],
                       xT[0, c, :, x], x_first_loaded[n])

        block = ctx.enter_context(nc.Block())

        @block.sync
        def _(sp):
            def load_pair(b, g, i, w, n, slots_new=False):
                for s in range(RAW):
                    if not slots_new:
                        sp.wait_ge(w_split, raw_free(unit(b, g, i + s)))
                    sp.dma_start(w_raw[:, s, :], w[g * GROUP + n * RAW + s, :, :],
                                 max_dma_last_dim=UNIT * 4).then_inc(w_loaded[s], 16)

            def load_group(b, g, after_first):
                with sp.Fori(after_first, ENC_UNITS // RAW) as n:
                    load_pair(b, g, n * RAW, w_enc, n)
                with sp.Fori(0, DEC_UNITS // RAW) as n:
                    load_pair(b, g, n * RAW + ENC_UNITS, w_dec, n)

            for _, _, raw, source, arrival in first_pieces():
                sp.dma_start(raw, source).then_inc(arrival, 16)
            load_pair(0, 0, RAW, w_enc, 1, slots_new=True)
            load_group(0, 0, 2)
            with sp.Fori(1, GROUPS) as g:
                load_group(0, g, 0)
            with sp.Fori(1, BLOCKS) as b:
                with sp.Fori(0, GROUPS) as g:
                    load_group(b, g, 0)
            for c in range(CHUNKS):
                for r in range(ROW_TILES):
                    sp.wait_ge(out_added, tiles_added(BLOCKS - 1, GROUPS - 1, c) + r + 1)
                    rows = slice((BLOCKS - 1) * N + r * P, (BLOCKS - 1) * N + (r + 1) * P)
                    cols = slice(c * N, (c + 1) * N)
                    sp.dma_start(out[rows, cols], out_sum[:, r, cols]).then_inc(last_stored, 16)
            sp.wait_ge(last_stored, 16 * CHUNKS * ROW_TILES)

        @block.gpsimd
        def _(pool):
            pool.sem_inc(out_free, 1)
            pool.wait_ge(w_split, 2 * SLOTS)
            pool.dma_start(b_dec_rows, b_dec.partition_broadcast(P)).then_inc(b_dec_loaded, 16)
            with pool.Fori(0, BLOCKS - 1) as b:
                rows = out[bass.ds(b * N, N), :].rearrange("(r p) d -> p r d", p=P)
                for c in range(CHUNKS):
                    cols = slice(c * N, (c + 1) * N)
                    pool.wait_ge(out_added, tiles_added(b, GROUPS - 1, c + 1))
                    pool.dma_start(rows[:, :, cols], out_sum[:, :, cols]).then_inc(out_stored, 16)
                pool.wait_ge(out_stored, b * (16 * CHUNKS) + 16 * CHUNKS)
                pool.sem_inc(out_free, 1)

        @block.scalar
        def _(act):
            def make_w_hi(b, g, i):
                s, r = i % SLOTS, i % RAW
                act.wait_ge(w_loaded[r], (unit(b, g, i) - r) * (16 // RAW))
                act.wait_ge(quarters, unit_used(unit(b, g, i) - SLOTS))
                act.activation(w_hi[:, s, :], w_raw[:, r, :], ACT.Copy).then_inc(w_hi_made, 1)

            def make_latent(b, g, i):
                s = i % LATENT_BANKS
                act.wait_ge(quarters, unit_used(unit(b, g, i)))
                act.wait_ge(latent_split, (b * GROUPS + g) * GROUP + i + 1)
                bias = b_enc_cols[:, bass.ds(g * GROUP + i, 1)]
                act.activation(latent[:, s, :], latent_ps[s][:, :], ACT.Relu, bias=bias)
                act.activation(f_hi[:, i, :], latent_ps[s][:, :], ACT.Relu, bias=bias)\
                    .then_inc(latent_made, 1)

            def load_x(b, c):
                if c > 0:
                    act.wait_ge(x_split, (b - 1) * X_UNITS + c)
                act.dma_start(x_raw, xT[b, c, :, :], max_dma_last_dim=UNIT * 4).then_inc(x_loaded, 16)

            def make_x_hi(b, c):
                act.wait_ge(x_loaded, (b - 1) * (16 * X_UNITS) + 16 * (c + 1))
                act.activation(x_part(x_hi, c), x_raw, ACT.Copy).then_inc(x_hi_made, 1)

            def group(b, g, prepare_x=False, ends=False):
                for i in range(G_UNITS):
                    if not (ends and i + SLOTS >= G_UNITS):
                        make_w_hi(b, g, i + SLOTS)
                    if i < ENC_UNITS:
                        make_latent(b, g, i)
                    if prepare_x:
                        c, odd = divmod(i - ENC_UNITS, PER_CHUNK)
                        if i == 0:
                            load_x(b + 1, 0)
                        elif c >= 0 and not odd:
                            make_x_hi(b + 1, c)
                        elif 0 <= c < X_UNITS - 1:
                            load_x(b + 1, c + 1)

            act.dma_start(b_enc_cols[:, :], b_enc[:, :]).then_inc(b_enc_loaded, 16)
            for hi, _, raw, _, arrival in first_pieces():
                act.wait_ge(arrival, 16)
                act.activation(hi, raw, ACT.Copy).then_inc(first_hi_made, 1)
            act.wait_ge(b_enc_loaded, 16)
            with act.Fori(0, BLOCKS - 1) as b:
                with act.Fori(0, GROUPS - 1) as g:
                    group(b, g)
                group(b, GROUPS - 1, prepare_x=True)
            with act.Fori(0, GROUPS - 1) as g:
                group(BLOCKS - 1, g)
            group(BLOCKS - 1, GROUPS - 1, ends=True)

        @block.vector
        def _(dve):
            def subtract(lo, raw, hi):
                return dve.tensor_tensor(lo, raw, hi.bitcast(f32), ALU.subtract)

            def make_w_lo(b, g, i):
                s, r = i % SLOTS, i % RAW
                dve.wait_ge(w_hi_made, unit(b, g, i) - SLOTS + 1)
                subtract(w_lo[:, s, :], w_raw[:, r, :], w_hi[:, s, :]).then_inc(w_split, 1)

            def split_latent(b, g, i):
                dve.wait_ge(latent_made, (b * GROUPS + g) * GROUP + i + 1)
                subtract(f_lo[:, i, :], latent[:, i % LATENT_BANKS, :], f_hi[:, i, :]).then_inc(latent_split, 1)

            def split_x(b, c):
                dve.wait_ge(x_hi_made, (b - 1) * X_UNITS + c + 1)
                subtract(x_part(x_lo, c), x_raw, x_part(x_hi, c)).then_inc(x_split, 1)

            def add_chunk(b, g, c, first):
                u = unit(b, g, ENC_UNITS + (c + 1) * PER_CHUNK - 1)
                cols = slice(c * N, (c + 1) * N)
                if first and c == 0:
                    dve.wait_ge(b_dec_loaded, 16)
                    dve.wait_ge(out_free, b + 1)
                for r in range(ROW_TILES):
                    dve.wait_ge(quarters, quarter_used(u, r))
                    onto = b_dec_rows[:, cols] if first else out_sum[:, r, cols]
                    dve.tensor_tensor(out_sum[:, r, cols], out_ps[r][:, :], onto, ALU.add)\
                        .then_inc(out_added, 1)

            def group(b, g, first=False, prepare_x=False, ends=False):
                for i in range(G_UNITS):
                    c, odd = divmod(i - ENC_UNITS, PER_CHUNK)
                    if c >= 0 and odd:
                        add_chunk(b, g, c, first)
                    if not (ends and i + SLOTS >= G_UNITS):
                        make_w_lo(b, g, i + SLOTS)
                    if i < ENC_UNITS:
                        split_latent(b, g, i)
                    elif prepare_x and not odd:
                        split_x(b + 1, c)

            dve.sem_inc(latent_split, LATENT_BANKS)
            dve.sem_inc(out_added, OUT_BANKS)
            for n, (hi, lo, raw, _, _) in enumerate(first_pieces()):
                dve.wait_ge(first_hi_made, n + 1)
                split = subtract(lo, raw, hi)
                if n % 2 == 1:
                    split.then_inc(first_split, 1)
                elif n == 2 * len(FIRST) - 2:
                    split.then_inc(w_split, SLOTS)
            with dve.Fori(0, BLOCKS - 1) as b:
                group(b, 0, first=True)
                with dve.Fori(1, GROUPS - 1) as g:
                    group(b, g)
                group(b, GROUPS - 1, prepare_x=True)
            group(BLOCKS - 1, 0, first=True)
            with dve.Fori(1, GROUPS - 1) as g:
                group(BLOCKS - 1, g)
            group(BLOCKS - 1, GROUPS - 1, ends=True)

        @block.tensor
        def _(pe):
            def products(ps, a_hi, a_lo, b_hi, b_lo, start, stop):
                pe.matmul(ps, a_hi, b_hi, start=start, stop=False)
                pe.matmul(ps, a_hi, b_lo, start=False, stop=False)
                return pe.matmul(ps, a_lo, b_hi, start=False, stop=stop)

            def encode_part(j, k_tiles):
                for k in k_tiles:
                    w = slice(k * P, (k + 1) * P)
                    last = products(latent_ps[j][:, :], w_hi[:, j, w], w_lo[:, j, w],
                                    x_hi[:, k, :], x_lo[:, k, :], k == 0, k == K_TILES - 1)
                return last

            def encode(b, g, i, j, first_block):
                pe.wait_ge(w_split, unit(b, g, i) + 1)
                if j == 0 and not first_block:
                    pe.wait_ge(x_split, b * X_UNITS)
                pe.wait_ge(latent_made, (b * GROUPS + g) * GROUP + i - LATENT_BANKS + 1)
                encode_part(j, range(K_TILES)).then_inc(quarters, QUARTERS)

            def decode(b, g, c, h):
                pe.wait_ge(w_split, unit(b, g, ENC_UNITS + c * PER_CHUNK + h) + 1)
                for r in range(ROW_TILES):
                    if h == 0:
                        pe.wait_ge(out_added, tiles_added(b, g, c) - OUT_BANKS + r + 1)
                    for t in range(DEC_TILES):
                        ft = h * DEC_TILES + t
                        if r == 0:
                            pe.wait_ge(latent_split, (b * GROUPS + g) * GROUP + ft + 1 + LATENT_BANKS)
                        w, rows = slice(t * N, (t + 1) * N), slice(r * P, (r + 1) * P)
                        last = products(out_ps[r][:, :], f_hi[:, ft, rows], f_lo[:, ft, rows],
                                        w_hi[:, h, w], w_lo[:, h, w], ft == 0, ft == GROUP - 1)
                    last.then_inc(quarters, 1)

            def group(b, g, after_first=0, first_block=False):
                with pe.Fori(after_first, ENC_UNITS // SLOTS) as n:
                    for j in range(SLOTS):
                        encode(b, g, n * SLOTS + j, j, first_block)
                with pe.Fori(0, CHUNKS) as c:
                    for h in range(PER_CHUNK):
                        decode(b, g, c, h)

            apart = len(FIRST) - 4
            order = [(n, j) for n in range(apart) for j in range(SLOTS)]
            order += [(n, j) for j in range(SLOTS) for n in range(apart, len(FIRST))]
            for n, j in order:
                pe.wait_ge(first_split, n + 1)
                last = encode_part(j, range(*FIRST[n]))
                if n == len(FIRST) - 1:
                    last.then_inc(quarters, QUARTERS)
            group(0, 0, after_first=1, first_block=True)
            with pe.Fori(1, GROUPS) as g:
                group(0, g, first_block=True)
            with pe.Fori(1, BLOCKS) as b:
                with pe.Fori(0, GROUPS) as g:
                    group(b, g)


def kernel(r_x, L0_rec_W_enc, L0_rec_b_enc, L0_rec_W_dec, L0_rec_b_dec):
    import numpy as np
    import concourse.bacc as bacc
    from concourse.bass_utils import run_bass_kernel_spmd

    def packed(a):
        return np.ascontiguousarray(a)

    x = np.asarray(r_x).reshape(BLOCKS, N, X_UNITS, X_TILES, P)
    we = np.asarray(L0_rec_W_enc).reshape(K_TILES, P, F // P, P)
    wd = np.asarray(L0_rec_W_dec).transpose(1, 0, 2).reshape(GROUPS, PER_CHUNK, DEC_TILES, P, CHUNKS, N)
    arrays = {
        "xT": packed(x.transpose(0, 2, 4, 3, 1)).reshape(BLOCKS, X_UNITS, P, UNIT),
        "w_enc": packed(we.transpose(2, 1, 0, 3)).reshape(GROUPS * ENC_UNITS, P, UNIT),
        "b_enc": packed(np.asarray(L0_rec_b_enc).reshape(F // P, P).T),
        "w_dec": packed(wd.transpose(0, 4, 1, 3, 2, 5)).reshape(GROUPS * DEC_UNITS, P, UNIT),
        "b_dec": packed(np.asarray(L0_rec_b_dec).reshape(D)),
    }
    nc = bacc.Bacc("TRN2", target_bir_lowering=False, num_devices=1)
    args = [nc.dram_tensor(name, a.shape, mybir.dt.from_np(a.dtype), kind="ExternalInput").ap()
            for name, a in arrays.items()]
    args.append(nc.dram_tensor("x_hat", [ROWS, D], mybir.dt.float32, kind="ExternalOutput").ap())
    build(nc, *args)
    got = run_bass_kernel_spmd(nc, [arrays], core_ids=[0])
    return got.results[0]["x_hat"].reshape(ROWS, LAYERS, WIDTH)
```
